# Optimizing a Trainium2 kernel written in Bass

```python
import numpy as np
import jax
import jax.numpy as jnp

def _softmax(x, axis=-1):
    return jax.nn.softmax(x, axis=axis)
def _gelu(x):
    return jax.nn.gelu(x, approximate=True)
def _silu(x):
    return jax.nn.silu(x)
def _sigmoid(x):
    return jax.nn.sigmoid(x)
def _layernorm(x, axis=-1, eps=1e-5):
    m = jnp.mean(x, axis=axis, keepdims=True)
    v = jnp.var(x, axis=axis, keepdims=True)
    return (x - m) / jnp.sqrt(v + eps)
def _scatter_add(tgt, idx, src, axis=0):
    return tgt.at[idx].add(src)
def _segment_sum(src, seg, n):
    return jax.ops.segment_sum(src, seg, n)

kernel_name = 'mk_conv_preact_d1_conv_nchw512_e32413'

def setup_inputs(seed: int = 0):
    np.random.seed(seed)
    _w = jnp.asarray
    def _rec_inputs():
        import jax
        import jax.numpy as jnp
        _gk = jax.random.key(seed)
        x = -8.268e-05 + 0.9999 * jax.random.normal(jax.random.fold_in(_gk, 1), (32, 512, 56, 56), jnp.float32)
        return x
    x = _rec_inputs()
    def _L0_conv_setup():
        import jax, jax.numpy as jnp
        import numpy as np
        EPS = 1e-05
        B, CIN, COUT, H, W = (32, 512, 512, 56, 56)
        K = 4
        A = 32
        key = jax.random.key(seed)
        ks = jax.random.split(key, 16)
        s = lambda fan: 1.0 / np.sqrt(fan)
        return {'x': jax.random.normal(ks[0], (B, CIN, H, W), jnp.float32), 'fc_w': jax.random.normal(ks[1], (A, CIN), jnp.float32) * s(CIN), 'abn_g': jnp.ones((A,), jnp.float32), 'abn_b': jnp.zeros((A,), jnp.float32), 'abn_m': jax.random.normal(ks[2], (A,), jnp.float32) * 0.1, 'abn_v': jax.random.uniform(ks[3], (A,), jnp.float32, 0.5, 1.5), 'ch_w': jax.random.normal(ks[4], (CIN, A), jnp.float32) * s(A), 'ch_b': jnp.zeros((CIN,), jnp.float32), 'fl_w': jax.random.normal(ks[5], (COUT, A), jnp.float32) * s(A), 'fl_b': jnp.zeros((COUT,), jnp.float32), 'kn_w': jax.random.normal(ks[6], (K, A), jnp.float32) * s(A), 'kn_b': jnp.zeros((K,), jnp.float32), 'weight': jax.random.normal(ks[7], (K, COUT, CIN), jnp.float32) * s(CIN), 'bn_g': jnp.ones((COUT,), jnp.float32), 'bn_b': jnp.zeros((COUT,), jnp.float32), 'bn_m': jax.random.normal(ks[8], (COUT,), jnp.float32) * 0.1, 'bn_v': jax.random.uniform(ks[9], (COUT,), jnp.float32, 0.5, 1.5)}
    _L0_conv_all = _L0_conv_setup()
    _L0_conv_in = {k: v for k, v in _L0_conv_all.items() if k in ('fc_w', 'abn_g', 'abn_b', 'abn_m', 'abn_v', 'ch_w', 'ch_b', 'fl_w', 'fl_b', 'kn_w', 'kn_b', 'weight', 'bn_g', 'bn_b', 'bn_m', 'bn_v', )}
    del _L0_conv_all

    return {
        "x": x,
        "L0_conv_fc_w": _L0_conv_in["fc_w"],
        "L0_conv_abn_g": _L0_conv_in["abn_g"],
        "L0_conv_abn_b": _L0_conv_in["abn_b"],
        "L0_conv_abn_m": _L0_conv_in["abn_m"],
        "L0_conv_abn_v": _L0_conv_in["abn_v"],
        "L0_conv_ch_w": _L0_conv_in["ch_w"],
        "L0_conv_ch_b": _L0_conv_in["ch_b"],
        "L0_conv_fl_w": _L0_conv_in["fl_w"],
        "L0_conv_fl_b": _L0_conv_in["fl_b"],
        "L0_conv_kn_w": _L0_conv_in["kn_w"],
        "L0_conv_kn_b": _L0_conv_in["kn_b"],
        "L0_conv_weight": _L0_conv_in["weight"],
        "L0_conv_bn_g": _L0_conv_in["bn_g"],
        "L0_conv_bn_b": _L0_conv_in["bn_b"],
        "L0_conv_bn_m": _L0_conv_in["bn_m"],
        "L0_conv_bn_v": _L0_conv_in["bn_v"],
    }

def reference(x, L0_conv_fc_w, L0_conv_abn_g, L0_conv_abn_b, L0_conv_abn_m, L0_conv_abn_v, L0_conv_ch_w, L0_conv_ch_b, L0_conv_fl_w, L0_conv_fl_b, L0_conv_kn_w, L0_conv_kn_b, L0_conv_weight, L0_conv_bn_g, L0_conv_bn_b, L0_conv_bn_m, L0_conv_bn_v):
    import jax
    import jax.numpy as jnp
    def _L0_conv_ref(x, fc_w, abn_g, abn_b, abn_m, abn_v, ch_w, ch_b, fl_w, fl_b, kn_w, kn_b, weight, bn_g, bn_b, bn_m, bn_v):
        import jax, jax.numpy as jnp
        import numpy as np
        EPS = 1e-05
        B, CIN, COUT, H, W = (32, 512, 512, 56, 56)
        K = 4
        A = 32
        pooled = jnp.mean(x, axis=(2, 3))
        h = pooled @ fc_w.T
        h = (h - abn_m) * (abn_g / jnp.sqrt(abn_v + EPS)) + abn_b
        h = jax.nn.relu(h)
        ch_att = jax.nn.sigmoid(h @ ch_w.T + ch_b)
        fl_att = jax.nn.sigmoid(h @ fl_w.T + fl_b)
        kn_att = jax.nn.softmax(h @ kn_w.T + kn_b, axis=1)
        agg_w = jnp.einsum('bk,koc->boc', kn_att, weight)
        xm = x * ch_att[:, :, None, None]
        y = jnp.einsum('bchw,boc->bohw', xm, agg_w)
        y = y * fl_att[:, :, None, None]
        inv = bn_g / jnp.sqrt(bn_v + EPS)
        y = (y - bn_m[None, :, None, None]) * inv[None, :, None, None] + bn_b[None, :, None, None]
        return y

    def _gn(v, G=32, eps=1e-5):
        B_, C_, H_, W_ = v.shape
        g = v.reshape(B_, G, C_ // G, H_, W_)
        m = jnp.mean(g, axis=(2, 3, 4), keepdims=True)
        s = jnp.var(g, axis=(2, 3, 4), keepdims=True)
        return ((g - m) / jnp.sqrt(s + eps)).reshape(v.shape)

    def _ln_c(v, eps=1e-6):
        m = jnp.mean(v, axis=1, keepdims=True)
        s = jnp.var(v, axis=1, keepdims=True)
        return (v - m) / jnp.sqrt(s + eps)

    def _ln_t(v, eps=1e-5):
        m = jnp.mean(v, axis=-1, keepdims=True)
        s = jnp.var(v, axis=-1, keepdims=True)
        return (v - m) / jnp.sqrt(s + eps)

    def _to_tokens(v):
        B_, C_, H_, W_ = v.shape
        return v.reshape(B_, C_, H_ * W_).transpose(0, 2, 1)
    def _from_tokens(t, like):
        B_, C_, H_, W_ = like.shape
        return t.transpose(0, 2, 1).reshape(B_, C_, H_, W_)

    x = x + _L0_conv_ref(_gn(x), L0_conv_fc_w, L0_conv_abn_g, L0_conv_abn_b, L0_conv_abn_m, L0_conv_abn_v, L0_conv_ch_w, L0_conv_ch_b, L0_conv_fl_w, L0_conv_fl_b, L0_conv_kn_w, L0_conv_kn_b, L0_conv_weight, L0_conv_bn_g, L0_conv_bn_b, L0_conv_bn_m, L0_conv_bn_v)
    return x


_drawn_inputs = setup_inputs


def setup_inputs(seed=0):
    import zlib

    import numpy as np

    out = dict(_drawn_inputs(seed))
    spreads = {'L0_conv_abn_g': (1.0, 0.6),
     'L0_conv_abn_b': (0.0, 0.8),
     'L0_conv_ch_b': (0.0, 0.8),
     'L0_conv_fl_b': (0.0, 0.8),
     'L0_conv_kn_b': (0.0, 0.566),
     'L0_conv_bn_g': (1.0, 0.2),
     'L0_conv_bn_b': (0.0, 0.1)}
    factors = {'L0_conv_fc_w': 8.0,
     'L0_conv_abn_m': 3.408,
     'L0_conv_abn_v': 8.0,
     'L0_conv_ch_w': 8.0,
     'L0_conv_fl_w': 8.0,
     'L0_conv_kn_w': 4.593}
    for name, (base, spread) in spreads.items():
        noise = np.random.default_rng([zlib.crc32(name.encode()), seed]).standard_normal(out[name].shape)
        drawn = base * np.exp(spread * noise) if base else spread * noise
        out[name] = jnp.asarray(drawn.astype(out[name].dtype))
    for name, factor in factors.items():
        out[name] = (out[name] * factor).astype(out[name].dtype)
    return out
```

```python
import concourse.bass as bass
from concourse import mybir
from contextlib import ExitStack

P = 128
GROUP = 16
HIDDEN = 32
KERNELS = 4
CHUNKS = 7
RING = 2 * CHUNKS
BANKS = 7
X_SCALE = 256.0
W_TOP = 2.0 ** 14
GN_EPS = 1e-5
BN_EPS = 1e-5


def columns(ct):
    sizes = [("fc", ct * HIDDEN), ("heads", (2 * ct + KERNELS) * HIDDEN), ("head_bias", 2 * ct + KERNELS),
             ("bn_v", ct), ("abn_v", HIDDEN), ("abn_g", HIDDEN), ("abn_b", HIDDEN), ("abn_m", HIDDEN),
             ("bn_g", ct), ("bn_b", ct), ("bn_m", ct), ("group", P), ("ident", P)]
    at, where = 0, {}
    for name, n in sizes:
        where[name] = (at, at + n)
        at += n
    return where, at


class Turn:

    def __init__(self, engine, i):
        self.engine, self.i, self.known = engine, i, {}

    def at(self, per_turn, c):
        if isinstance(self.i, int):
            return self.i * per_turn + c
        if per_turn not in self.known:
            self.known[per_turn] = self.engine.snap(self.i * per_turn)
        return self.known[per_turn] + c


def build(nc, x, wt, par, out):
    f32, f16 = mybir.dt.float32, mybir.dt.float16
    ALU, ACT, AX = mybir.AluOpType, mybir.ActivationFunctionType, mybir.AxisListType
    B, C, HW = x.shape
    CT = C // P
    COLS = HW // CHUNKS
    TURNS = B // 2
    HEADS = 2 * CT + KERNELS
    where, n_par = columns(CT)

    x_d = x.rearrange("b (t p) n -> b p t n", p=P)
    out_d = out.rearrange("b (t p) n -> b p t n", p=P)

    ctx = ExitStack()
    with ctx:
        def sb(name, shape, dt=f32):
            return ctx.enter_context(nc.sbuf_tensor(name, shape, dt))

        def sem(name):
            return ctx.enter_context(nc.semaphore(name))

        xs = sb("x_ring", [P, RING, CT, COLS])
        xn = sb("x_norm", [P, 2, CT, COLS])
        xhi = sb("x_hi", [P, 2, CT, COLS], f16)
        xlo = sb("x_lo", [P, 2, CT, COLS], f16)
        y = sb("y", [P, 2, CT, COLS])
        w = sb("weight", [P, KERNELS, CT, C])
        mix = sb("mixed_weight", [P, CT, C])
        whi = sb("w_hi", [P, 2, CT, C], f16)
        wlo = sb("w_lo", [P, 2, CT, C], f16)
        pa = sb("params", [P, n_par])
        ones = sb("ones", [P, P])
        bst = sb("chunk_stats", [P, 2, CT, CHUNKS, 6])
        mv = sb("mean_var", [P, CT, 2])
        gm = sb("group_mean", [P, CT])
        dev = sb("mean_deviation", [P, CT])
        spread = sb("spread", [P, CT])
        ve = sb("var_eps", [P, CT])
        ln = sb("ln_var", [P, CT])
        r0 = sb("rstd_guess", [P, CT])
        tmp = sb("newton", [P, CT])
        rstd = sb("rstd", [P, CT])
        nscale = sb("norm_scale", [P, 2, CT])
        nbias = sb("norm_bias", [P, 2, CT])
        pooled = sb("pooled", [P, CT])
        fcp = sb("fc_pooled", [P, CT, HIDDEN])
        hid = sb("hidden", [P, HIDDEN])
        prod = sb("head_products", [P, HEADS, HIDDEN])
        z = sb("logits", [P, HEADS])
        kmax = sb("kernel_max", [P, 1])
        ez = sb("exp_logits", [P, HEADS])
        sig = sb("sigmoids", [P, 2 * CT])
        ksum = sb("kernel_sum", [P, 1])
        katt = sb("kernel_att", [P, KERNELS])
        oscale = sb("out_scale", [P, 2, CT])
        V36 = CT + HIDDEN
        v_all = sb("bn_vars", [P, V36])
        ln_all = sb("bn_ln", [P, V36])
        r_all = sb("bn_guess", [P, V36])
        t_all = sb("bn_newton", [P, V36])
        rs_all = sb("bn_rstd", [P, V36])
        inv = sb("bn_scale", [P, CT])
        arow = sb("abn_scale", [P, HIDDEN])
        obias = sb("out_bias", [P, CT])
        wmax = sb("weight_max", [P, KERNELS])
        wmax1 = sb("weight_max_1", [P, 1])
        wtop = sb("weight_top", [1, 1])
        wall = sb("weight_top_all", [P, 1])
        wscale = sb("weight_scale", [P, 1])
        unscale = sb("weight_unscale", [P, 1])

        acc = [ctx.enter_context(nc.psum_tensor(f"product_{k}", [P, 512], f32)) for k in range(BANKS)]
        small = ctx.enter_context(nc.psum_tensor("small", [P, 512], f32))
        gmean_p, gvar_p, hid_p = small[:, 0:CT], small[:, 8:8 + CT], small[:, 16:16 + HIDDEN]
        top_row, top_all = small[0:1, 64:64 + P], small[:, 200:201]

        def p_(name):
            return pa[:, where[name][0]:where[name][1]]

        params_in = sem("params_in")
        weight_in = [sem(f"weight_in_{k}") for k in range(KERNELS)]
        chunk_in = [sem(f"chunk_in_{k}") for k in range(RING)]
        chunk_out = [sem(f"chunk_out_{k}") for k in range(RING)]
        order = sem("vector_order")
        stats_done = sem("stats_done")
        wmax_ready = sem("wmax_ready")
        wtop_ready = sem("wtop_ready")
        const_ready = sem("const_ready")
        means_ready = sem("means_ready")
        spread_ready = sem("spread_ready")
        var_ready = sem("var_ready")
        norm_ready = sem("norm_ready")
        pooled_ready = sem("pooled_ready")
        logits_ready = sem("logits_ready")
        att_ready = sem("att_ready")
        mix_ready = sem("mix_ready")
        wlo_ready = sem("wlo_ready")
        lo_ready = sem("lo_ready")
        add_done = sem("add_done")
        ln_ready = sem("ln_ready")
        guess_ready = sem("guess_ready")
        exp_ready = sem("exp_ready")
        mix0_ready = sem("mix0_ready")
        whi_ready = sem("whi_ready")
        xn_ready = sem("xn_ready")
        hi_ready = sem("hi_ready")
        evac_done = sem("evac_done")
        mm_done = sem("mm_done")
        top_moved = sem("top_moved")
        gmean_done = sem("gmean_done")
        gvar_done = sem("gvar_done")
        hid_done = sem("hid_done")

        block = ctx.enter_context(nc.Block())

        STATS_AHEAD, NORM_AHEAD, SPLIT_AHEAD = 12, 2, 1

        @block.sync
        def _(sp):
            def load(b, slot):
                n = slot % CHUNKS
                sp.dma_start(xs[:, slot], x_d[b, :, :, n * COLS:(n + 1) * COLS]).then_inc(chunk_in[slot], 16)

            sp.dma_start(pa[:, :], par).then_inc(params_in, 16)
            for slot in range(CHUNKS):
                load(0, slot)
            for k in range(KERNELS):
                sp.dma_start(w[:, k], wt[:, k]).then_inc(weight_in[k], 16)
            for slot in range(CHUNKS, RING):
                load(1, slot)

            def body(i, last):
                turn = Turn(sp, i)
                for s in range(RING):
                    n = s % CHUNKS
                    b = 2 * i + s // CHUNKS
                    sp.wait_ge(add_done, turn.at(2 * RING, 4 + 2 * (s + 1)))
                    sp.dma_start(out_d[b, :, :, n * COLS:(n + 1) * COLS], xs[:, s]).then_inc(chunk_out[s], 16)
                    if not last:
                        sp.wait_ge(chunk_out[s], turn.at(16, 16))
                        load(b + 2, s)
            with sp.Fori(0, TURNS - 1) as i:
                body(i, False)
            body(TURNS - 1, True)
            for s in range(RING):
                sp.wait_ge(chunk_out[s], 16 * TURNS)

        @block.scalar
        def _(act):
            def norm(turn, f, t):
                u = f // CHUNKS % 2
                if t == 0:
                    act.wait_ge(norm_ready, turn.at(2, f // CHUNKS + 1))
                    if f >= 2 or not isinstance(turn.i, int):
                        act.wait_ge(lo_ready, turn.at(RING, f - 1))
                ins = nc.scalar.activation(xn[:, f % 2, t], xs[:, f % RING, t], ACT.Identity,
                                           bias=nbias[:, u, t:t + 1], scale=nscale[:, u, t:t + 1])
                if t == CT - 1:
                    ins.then_inc(xn_ready, 1)

            def split(turn, f):
                act.wait_ge(xn_ready, turn.at(RING, f + 1))
                if f >= 2 or not isinstance(turn.i, int):
                    act.wait_ge(mm_done, turn.at(4 * RING, 4 * (f - 1)))
                nc.scalar.activation(xhi[:, f % 2], xn[:, f % 2], ACT.Copy).then_inc(hi_ready, 1)

            def evacuate(turn, s, t):
                k = 4 * s + t
                u = s // CHUNKS
                act.wait_ge(mm_done, turn.at(4 * RING, k + 1))
                if t % 2 == 0:
                    act.wait_ge(add_done, turn.at(2 * RING, 2 * s + t // 2 + 1))
                nc.scalar.activation(y[:, s % 2, t], acc[k % BANKS][:, 0:COLS], ACT.Identity,
                                     bias=obias[:, t:t + 1], scale=oscale[:, u, t:t + 1]).then_inc(evac_done, 1)

            def guess(turn, b):
                act.wait_ge(var_ready, turn.at(2, b + 1))
                nc.scalar.activation(ln[:, :], ve[:, :], ACT.Ln).then_inc(ln_ready, 1)
                act.wait_ge(ln_ready, turn.at(2, b + 2))
                nc.scalar.activation(r0[:, :], ln[:, :], ACT.Exp, scale=-0.5).then_inc(guess_ready, 1)

            def exponentials(turn, b):
                act.wait_ge(logits_ready, turn.at(2, b + 1))
                nc.scalar.activation(ez[:, :], z[:, :], ACT.Exp, scale=-1.0).then_inc(exp_ready, 1)

            def first_mix(turn, b):
                act.wait_ge(att_ready, turn.at(2, b + 1))
                if b or not isinstance(turn.i, int):
                    act.wait_ge(wlo_ready, turn.at(2, b))
                nc.scalar.activation(mix[:, :, :], w[:, 0], ACT.Copy, scale=katt[:, 0:1]).then_inc(mix0_ready, 1)

            def split_weight(turn, b):
                act.wait_ge(mix_ready, turn.at(2, b + 1))
                for t in range(CT):
                    ins = nc.scalar.activation(whi[:, b % 2, t], mix[:, t], ACT.Copy, scale=sig[:, t:t + 1])
                ins.then_inc(whi_ready, 1)

            act.preload_act_table_set("natural_log_exp_and_others")
            act.sem_inc(evac_done, BANKS)
            start = Turn(act, 0)
            act.wait_ge(const_ready, 2)
            nc.scalar.activation(ln_all[:, :], v_all[:, :], ACT.Ln).then_inc(ln_ready, 1)
            act.wait_ge(ln_ready, 1)
            nc.scalar.activation(r_all[:, :], ln_all[:, :], ACT.Exp, scale=-0.5).then_inc(guess_ready, 1)
            guess(start, 0)
            for t in range(CT):
                norm(start, 0, t)
            split(start, 0)
            exponentials(start, 0)
            for t in range(CT):
                norm(start, 1, t)
            act.wait_ge(weight_in[0], 16)
            first_mix(start, 0)
            split_weight(start, 0)

            def body(i, last):
                turn = Turn(act, i)
                for s in range(RING):
                    n, b = s % CHUNKS, s // CHUNKS + 1
                    prepare = not (last and b == 2)
                    for t in range(CT):
                        if t == 0 and not (last and s + SPLIT_AHEAD >= RING):
                            split(turn, s + SPLIT_AHEAD)
                        evacuate(turn, s, t)
                        if not (last and s + NORM_AHEAD >= RING):
                            norm(turn, s + NORM_AHEAD, t)
                        if prepare:
                            if (n, t) == (3, 1):
                                guess(turn, b)
                            if (n, t) == (4, 2):
                                exponentials(turn, b)
                            if (n, t) == (5, 0):
                                first_mix(turn, b)
                            if (n, t) == (6, 0):
                                split_weight(turn, b)
            with act.Fori(0, TURNS - 1) as i:
                body(i, False)
            body(TURNS - 1, True)

        @block.vector
        def _(dve):
            done = [0]
            steps = []

            def step(ins):
                done[0] += 1
                ins.then_inc(order, 1)

            def after(turn):
                dve.wait_ge(order, turn.at(2 * STEPS, done[0]))

            STEPS = 22 + CT

            def stats(turn, f, t):
                if t == 0:
                    dve.wait_ge(chunk_in[f % RING], turn.at(16, 16 * (f // RING + 1)))
                ins = nc.vector.bn_stats(bst[:, f // CHUNKS % 2, t, f % CHUNKS], xs[:, f % RING, t])
                if t == CT - 1:
                    ins.then_inc(stats_done, 1)

            def split(turn, f):
                dve.wait_ge(hi_ready, turn.at(RING, f + 1))
                nc.vector.tensor_tensor(xlo[:, f % 2], xn[:, f % 2], xhi[:, f % 2], ALU.subtract).then_inc(lo_ready, 1)

            def add(turn, s, half):
                dve.wait_ge(evac_done, turn.at(4 * RING, BANKS + 4 * s + 2 * half + 2))
                two = slice(2 * half, 2 * half + 2)
                nc.vector.tensor_tensor(xs[:, s, two], xs[:, s, two], y[:, s % 2, two], ALU.add).then_inc(add_done, 1)

            def newton(turn, r, guess_, v, t):
                step(nc.vector.tensor_tensor(t, guess_, guess_, ALU.mult))
                after(turn)
                step(nc.vector.tensor_tensor(t, t, v, ALU.mult))
                after(turn)
                step(nc.vector.tensor_scalar(t, t, -0.5, 1.5, ALU.mult, ALU.add))
                after(turn)
                step(nc.vector.tensor_tensor(r, guess_, t, ALU.mult))
                after(turn)


            def stats_complete(turn, b):
                dve.wait_ge(stats_done, turn.at(RING, CHUNKS * (b + 1)))

            def channel_means(turn, b):
                for t in range(CT):
                    ins = nc.vector.bn_aggr(mv[:, t], bst[:, b % 2, t].rearrange("p c k -> p (c k)"))
                ins.then_inc(means_ready, 1)

            def group_spread(turn, b):
                dve.wait_ge(means_ready, turn.at(2, b + 1))
                dve.wait_ge(gmean_done, turn.at(2, b + 1))
                step(nc.vector.tensor_tensor(dev[:, :], mv[:, :, 0], gmean_p, ALU.subtract))
                step(nc.vector.tensor_copy(gm[:, :], gmean_p))
                after(turn)
                step(nc.vector.tensor_tensor(spread[:, :], dev[:, :], dev[:, :], ALU.mult))
                after(turn)
                nc.vector.tensor_tensor(spread[:, :], spread[:, :], mv[:, :, 1], ALU.add).then_inc(spread_ready, 1)

            def group_var(turn, b):
                dve.wait_ge(gvar_done, turn.at(2, b + 1))
                nc.vector.tensor_scalar(ve[:, :], gvar_p, GN_EPS, None, ALU.add).then_inc(var_ready, 1)

            def norms(turn, b):
                u = b % 2
                dve.wait_ge(guess_ready, turn.at(2, b + 2))
                newton(turn, rstd[:, :], r0[:, :], ve[:, :], tmp[:, :])
                step(nc.vector.tensor_scalar(nscale[:, u], rstd[:, :], X_SCALE, None, ALU.mult))
                step(nc.vector.tensor_tensor(pooled[:, :], dev[:, :], rstd[:, :], ALU.mult))
                after(turn)
                nc.vector.scalar_tensor_tensor(out=nbias[:, u], in0=gm[:, :], scalar=-1.0, in1=nscale[:, u],
                                               op0=ALU.mult, op1=ALU.mult).then_inc(norm_ready, 1)
                nc.vector.tensor_tensor(fcp[:, :, :], p_("fc").rearrange("p (t a) -> p t a", t=CT),
                                        pooled[:, :].unsqueeze(2).to_broadcast([P, CT, HIDDEN]),
                                        ALU.mult).then_inc(pooled_ready, 1)

            def logits(turn, b):
                dve.wait_ge(hid_done, turn.at(2, b + 1))
                step(nc.vector.tensor_tensor(hid[:, :], hid_p, p_("abn_m"), ALU.subtract))
                after(turn)
                step(nc.vector.tensor_tensor(hid[:, :], hid[:, :], arow[:, :], ALU.mult))
                after(turn)
                step(nc.vector.tensor_tensor(hid[:, :], hid[:, :], p_("abn_b"), ALU.add))
                after(turn)
                step(nc.vector.scalar_tensor_tensor(out=prod[:, :, :],
                                                    in0=hid[:, :].unsqueeze(1).to_broadcast([P, HEADS, HIDDEN]),
                                                    scalar=0.0, in1=p_("heads").rearrange("p (j a) -> p j a", a=HIDDEN),
                                                    op0=ALU.max, op1=ALU.mult))
                after(turn)
                step(nc.vector.tensor_reduce(z[:, :], prod[:, :, :], AX.X, ALU.add))
                after(turn)
                step(nc.vector.tensor_tensor(z[:, :], z[:, :], p_("head_bias"), ALU.add))
                after(turn)
                step(nc.vector.reduce_max(kmax[:, :], z[:, 2 * CT:HEADS], AX.X))
                after(turn)
                nc.vector.tensor_scalar(z[:, 2 * CT:HEADS], z[:, 2 * CT:HEADS], kmax[:, 0:1], -1.0,
                                        ALU.subtract, ALU.mult).then_inc(logits_ready, 1)

            def attentions(turn, b):
                dve.wait_ge(exp_ready, turn.at(2, b + 1))
                step(nc.vector.tensor_scalar(sig[:, :], ez[:, 0:2 * CT], 1.0, None, ALU.add))
                step(nc.vector.reduce_sum(ksum[:, :], ez[:, 2 * CT:HEADS], AX.X))
                after(turn)
                step(nc.vector.reciprocal(sig[:, :], sig[:, :]))
                step(nc.vector.reciprocal(ksum[:, :], ksum[:, :]))
                after(turn)
                step(nc.vector.tensor_tensor(oscale[:, b % 2], sig[:, CT:2 * CT], inv[:, :], ALU.mult))
                nc.vector.tensor_scalar(katt[:, :], ez[:, 2 * CT:HEADS], ksum[:, 0:1], wscale[:, 0:1],
                                        ALU.mult, ALU.mult).then_inc(att_ready, 1)

            def mix_kernel(turn, b, k):
                if k == 1:
                    dve.wait_ge(att_ready, turn.at(2, b + 1))
                    dve.wait_ge(mix0_ready, turn.at(2, b + 1))
                else:
                    after(turn)
                ins = nc.vector.scalar_tensor_tensor(out=mix[:, :, :], in0=w[:, k], scalar=katt[:, k:k + 1],
                                                     in1=mix[:, :, :], op0=ALU.mult, op1=ALU.add)
                if k == KERNELS - 1:
                    ins.then_inc(mix_ready, 1)
                else:
                    step(ins)

            def split_weight(turn, b, t):
                if t == 0:
                    dve.wait_ge(mix_ready, turn.at(2, b + 1))
                    dve.wait_ge(whi_ready, turn.at(2, b + 1))
                ins = nc.vector.scalar_tensor_tensor(out=wlo[:, b % 2, t], in0=mix[:, t], scalar=sig[:, t:t + 1],
                                                     in1=whi[:, b % 2, t], op0=ALU.mult, op1=ALU.subtract)
                if t == CT - 1:
                    ins.then_inc(wlo_ready, 1)
                else:
                    step(ins)

            start = Turn(dve, 0)
            dve.sem_inc(add_done, 4)
            nc.vector.memset(ones[:, :], 1.0).then_inc(const_ready, 1)
            dve.wait_ge(params_in, 16)
            nc.vector.tensor_scalar(v_all[:, :], pa[:, where["bn_v"][0]:where["abn_v"][1]], BN_EPS, None,
                                    ALU.add).then_inc(const_ready, 1)
            dve.wait_ge(guess_ready, 1)
            newton(start, rs_all[:, :], r_all[:, :], v_all[:, :], t_all[:, :])
            step(nc.vector.tensor_tensor(inv[:, :], p_("bn_g"), rs_all[:, 0:CT], ALU.mult))
            step(nc.vector.tensor_tensor(arow[:, :], p_("abn_g"), rs_all[:, CT:V36], ALU.mult))
            after(start)
            step(nc.vector.tensor_tensor(obias[:, :], p_("bn_m"), inv[:, :], ALU.mult))
            after(start)
            step(nc.vector.tensor_tensor(obias[:, :], p_("bn_b"), obias[:, :], ALU.subtract))
            for f in range(CHUNKS):
                for t in range(CT):
                    stats(start, f, t)
            stats_complete(start, 0)
            channel_means(start, 0)
            group_spread(start, 0)
            group_var(start, 0)
            norms(start, 0)
            logits(start, 0)
            for k in range(KERNELS):
                dve.wait_ge(weight_in[k], 16)
                step(nc.vector.tensor_reduce(wmax[:, k:k + 1], w[:, k].rearrange("p t o -> p (t o)"), AX.X, ALU.max,
                                             apply_absolute_value=True))
            after(start)
            nc.vector.reduce_max(wmax1[:, :], wmax[:, :], AX.X).then_inc(wmax_ready, 1)
            dve.wait_ge(top_moved, 1)
            nc.vector.reduce_max(wtop[:, :], top_row, AX.X).then_inc(wtop_ready, 1)
            dve.wait_ge(top_moved, 2)
            step(nc.vector.tensor_scalar(wall[:, :], top_all, 1e-30, None, ALU.max))
            after(start)
            step(nc.vector.reciprocal(wscale[:, :], wall[:, :]))
            step(nc.vector.tensor_scalar(unscale[:, :], wall[:, :], 1.0 / (W_TOP * X_SCALE), None, ALU.mult))
            after(start)
            step(nc.vector.tensor_scalar(wscale[:, :], wscale[:, :], W_TOP, None, ALU.mult))
            step(nc.vector.tensor_scalar(inv[:, :], inv[:, :], unscale[:, 0:1], None, ALU.mult))
            after(start)
            attentions(start, 0)
            split(start, 0)
            for k in range(1, KERNELS):
                mix_kernel(start, 0, k)
            for t in range(CT):
                split_weight(start, 0, t)
            for f in range(CHUNKS, STATS_AHEAD):
                for t in range(CT):
                    stats(start, f, t)
            before = done[0]

            def body(i, last):
                turn = Turn(dve, i)
                done[0] = before
                for s in range(RING):
                    n, b = s % CHUNKS, s // CHUNKS + 1
                    prepare = not (last and b == 2)
                    take = not (last and s + STATS_AHEAD >= RING)
                    for t in range(CT):
                        if t == 0:
                            if take:
                                stats(turn, s + STATS_AHEAD, 0)
                                stats(turn, s + STATS_AHEAD, 1)
                            if not (last and s + SPLIT_AHEAD >= RING):
                                split(turn, s + SPLIT_AHEAD)
                        if prepare:
                            if (n, t) == (2, 2):
                                group_spread(turn, b)
                            if (n, t) == (3, 1):
                                group_var(turn, b)
                            if (n, t) == (3, 3):
                                norms(turn, b)
                            if (n, t) == (4, 2):
                                logits(turn, b)
                            if (n, t) == (5, 0):
                                attentions(turn, b)
                            if n == 5 and t >= 1:
                                mix_kernel(turn, b, t)
                            if n == 6 and t >= 1:
                                for j in {1: (0, 1), 2: (2,), 3: (3,)}[t]:
                                    split_weight(turn, b, j)
                        if t == 2 and take:
                            stats(turn, s + STATS_AHEAD, 2)
                            stats(turn, s + STATS_AHEAD, 3)
                        if prepare and (n, t) == (1, 3):
                            stats_complete(turn, b)
                        if t % 2:
                            add(turn, s, t // 2)
                        if prepare and (n, t) == (1, 3):
                            channel_means(turn, b)
                    if s == CHUNKS - 1:
                        assert done[0] - before == STEPS, done[0] - before
            with dve.Fori(0, TURNS - 1) as i:
                body(i, False)
            body(TURNS - 1, True)

        @block.tensor
        def _(pe):
            def group_mean(turn, b):
                pe.wait_ge(means_ready, turn.at(2, b + 1))
                nc.tensor.matmul(gmean_p, p_("group"), mv[:, :, 0], start=True, stop=True).then_inc(gmean_done, 1)

            def group_var(turn, b):
                pe.wait_ge(spread_ready, turn.at(2, b + 1))
                nc.tensor.matmul(gvar_p, p_("group"), spread[:, :], start=True, stop=True).then_inc(gvar_done, 1)

            def hidden(turn, b):
                pe.wait_ge(pooled_ready, turn.at(2, b + 1))
                for t in range(CT):
                    ins = nc.tensor.matmul(hid_p, ones[:, :], fcp[:, t], start=(t == 0), stop=(t == CT - 1))
                ins.then_inc(hid_done, 1)

            start = Turn(pe, 0)
            pe.wait_ge(params_in, 16)
            pe.wait_ge(const_ready, 1)
            group_mean(start, 0)
            group_var(start, 0)
            hidden(start, 0)
            pe.wait_ge(wmax_ready, 1)
            nc.tensor.matmul(top_row, wmax1[:, 0:1], p_("ident"), start=True, stop=True).then_inc(top_moved, 1)
            pe.wait_ge(wtop_ready, 1)
            nc.tensor.matmul(top_all, ones[0:1, :], wtop[0:1, 0:1], start=True, stop=True).then_inc(top_moved, 1)

            def product(turn, s, o):
                k = 4 * s + o
                u = s // CHUNKS
                if o == 0:
                    if s % CHUNKS == 0:
                        pe.wait_ge(wlo_ready, turn.at(2, u + 1))
                    pe.wait_ge(lo_ready, turn.at(RING, s + 1))
                pe.wait_ge(evac_done, turn.at(4 * RING, k + 1))
                bank = acc[k % BANKS][:, 0:COLS]
                cols = slice(o * P, (o + 1) * P)
                for t in range(CT):
                    hi, lo = xhi[:, s % 2, t], xlo[:, s % 2, t]
                    nc.tensor.matmul(bank, whi[:, u, t, cols], hi, start=(t == 0), stop=False)
                    nc.tensor.matmul(bank, whi[:, u, t, cols], lo, start=False, stop=False)
                    ins = nc.tensor.matmul(bank, wlo[:, u, t, cols], hi, start=False, stop=(t == CT - 1))
                ins.then_inc(mm_done, 1)

            def body(i, last):
                turn = Turn(pe, i)
                for s in range(RING):
                    n, b = s % CHUNKS, s // CHUNKS + 1
                    prepare = not (last and b == 2)
                    for o in range(CT):
                        product(turn, s, o)
                        if prepare and (n, o) == (2, 1):
                            group_mean(turn, b)
                        if prepare and (n, o) == (3, 0):
                            group_var(turn, b)
                        if prepare and (n, o) == (4, 1):
                            hidden(turn, b)
            with pe.Fori(0, TURNS - 1) as i:
                body(i, False)
            body(TURNS - 1, True)


def kernel(x, L0_conv_fc_w, L0_conv_abn_g, L0_conv_abn_b, L0_conv_abn_m, L0_conv_abn_v, L0_conv_ch_w, L0_conv_ch_b,
           L0_conv_fl_w, L0_conv_fl_b, L0_conv_kn_w, L0_conv_kn_b, L0_conv_weight, L0_conv_bn_g, L0_conv_bn_b,
           L0_conv_bn_m, L0_conv_bn_v):
    import numpy as np
    import concourse.bacc as bacc
    from concourse.bass_utils import run_bass_kernel_spmd

    x = np.asarray(x)
    B, C, H, W = x.shape
    CT = C // P
    where, n_par = columns(CT)
    f = np.float32
    par = np.zeros((P, n_par), f)

    def put(name, a):
        a = np.asarray(a)
        lo, hi = where[name]
        par[:, lo:hi] = a.reshape(-1, hi - lo)

    def by_channel(a):
        a = np.asarray(a)
        return np.swapaxes(a.reshape(CT, P, *a.shape[1:]), 0, 1)

    def everywhere(a):
        a = np.asarray(a)
        return np.broadcast_to(a, (P, *a.shape))

    put("fc", by_channel(np.asarray(L0_conv_fc_w).T))
    put("heads", np.concatenate([by_channel(L0_conv_ch_w), by_channel(L0_conv_fl_w), everywhere(L0_conv_kn_w)], 1))
    put("head_bias", np.concatenate([by_channel(L0_conv_ch_b), by_channel(L0_conv_fl_b), everywhere(L0_conv_kn_b)], 1))
    for name, a in (("g", L0_conv_abn_g), ("b", L0_conv_abn_b), ("m", L0_conv_abn_m), ("v", L0_conv_abn_v)):
        put("abn_" + name, everywhere(a))
    for name, a in (("g", L0_conv_bn_g), ("b", L0_conv_bn_b), ("m", L0_conv_bn_m), ("v", L0_conv_bn_v)):
        put("bn_" + name, by_channel(a))
    put("group", np.kron(np.eye(P // GROUP, dtype=f), np.full((GROUP, GROUP), 1.0 / GROUP, f)))
    put("ident", np.eye(P, dtype=f))
    wt = np.ascontiguousarray(np.asarray(L0_conv_weight).reshape(KERNELS, C, CT, P).transpose(3, 0, 2, 1))

    nc = bacc.Bacc("TRN2", target_bir_lowering=False, num_devices=1)
    arrays = {"x": np.ascontiguousarray(x.reshape(B, C, H * W)), "wt": wt, "par": par}
    args = [nc.dram_tensor(n, a.shape, mybir.dt.from_np(a.dtype), kind="ExternalInput").ap() for n, a in arrays.items()]
    out = nc.dram_tensor("out", (B, C, H * W), mybir.dt.float32, kind="ExternalOutput").ap()
    build(nc, *args, out)
    r = run_bass_kernel_spmd(nc, [arrays], core_ids=[0])
    return r.results[0]["out"].reshape(B, C, H, W)
```

```python
import concourse.bass as bass
from concourse import mybir
from contextlib import ExitStack

P = 128
GROUP = 16
HIDDEN = 32
KERNELS = 4
CHUNKS = 7
RING = 2 * CHUNKS
BANKS = 7
X_SCALE = 256.0
W_TOP = 2.0 ** 15
GN_EPS = 1e-5
BN_EPS = 1e-5


def columns(ct):
    sizes = [("fc", ct * HIDDEN), ("heads", (2 * ct + KERNELS) * HIDDEN), ("head_bias", 2 * ct + KERNELS),
             ("bn_v", ct), ("abn_v", HIDDEN), ("abn_g", HIDDEN), ("abn_b", HIDDEN), ("abn_m", HIDDEN),
             ("bn_g", ct), ("bn_b", ct), ("bn_m", ct), ("group", P), ("ident", P)]
    at, where = 0, {}
    for name, n in sizes:
        where[name] = (at, at + n)
        at += n
    return where, at


class Turn:

    def __init__(self, engine, i):
        self.engine, self.i, self.known = engine, i, {}

    def at(self, per_turn, c):
        if isinstance(self.i, int):
            return self.i * per_turn + c
        if per_turn not in self.known:
            self.known[per_turn] = self.engine.snap(self.i * per_turn)
        return self.known[per_turn] + c


def build(nc, x, wt, par, out):
    f32, f16 = mybir.dt.float32, mybir.dt.float16
    ALU, ACT, AX = mybir.AluOpType, mybir.ActivationFunctionType, mybir.AxisListType
    B, C, HW = x.shape
    CT = C // P
    COLS = HW // CHUNKS
    TURNS = B // 2
    HEADS = 2 * CT + KERNELS
    where, n_par = columns(CT)

    x_d = x.rearrange("b (t p) n -> b p t n", p=P)
    out_d = out.rearrange("b (t p) n -> b p t n", p=P)

    ctx = ExitStack()
    with ctx:
        def sb(name, shape, dt=f32):
            return ctx.enter_context(nc.sbuf_tensor(name, shape, dt))

        def sem(name):
            return ctx.enter_context(nc.semaphore(name))

        xs = sb("x_ring", [P, RING, CT, COLS])
        xn = sb("x_norm", [P, 2, CT, COLS])
        xhi = sb("x_hi", [P, 2, CT, COLS], f16)
        xlo = sb("x_lo", [P, 2, CT, COLS], f16)
        y = sb("y", [P, 2, CT, COLS])
        w = sb("weight", [P, KERNELS, CT, C])
        mix = sb("mixed_weight", [P, CT, C])
        whi = sb("w_hi", [P, 2, CT, C], f16)
        wlo = sb("w_lo", [P, 2, CT, C], f16)
        pa = sb("params", [P, n_par])
        ones = sb("ones", [P, P])
        bst = sb("chunk_stats", [P, 2, CT, CHUNKS, 6])
        mv = sb("mean_var", [P, CT, 2])
        gm = sb("group_mean", [P, CT])
        dev = sb("mean_deviation", [P, CT])
        spread = sb("spread", [P, CT])
        ve = sb("var_eps", [P, CT])
        ln = sb("ln_var", [P, CT])
        r0 = sb("rstd_guess", [P, CT])
        tmp = sb("newton", [P, CT])
        rstd = sb("rstd", [P, CT])
        nscale = sb("norm_scale", [P, 2, CT])
        nbias = sb("norm_bias", [P, 2, CT])
        pooled = sb("pooled", [P, CT])
        fcp = sb("fc_pooled", [P, CT, HIDDEN])
        hid = sb("hidden", [P, HIDDEN])
        prod = sb("head_products", [P, HEADS, HIDDEN])
        z = sb("logits", [P, HEADS])
        kmax = sb("kernel_max", [P, 1])
        ez = sb("exp_logits", [P, HEADS])
        sig = sb("sigmoids", [P, 2 * CT])
        ksum = sb("kernel_sum", [P, 1])
        katt = sb("kernel_att", [P, KERNELS])
        catt = sb("channel_att_scaled", [P, CT])
        oscale = sb("out_scale", [P, 2, CT])
        V36 = CT + HIDDEN
        v_all = sb("bn_vars", [P, V36])
        ln_all = sb("bn_ln", [P, V36])
        r_all = sb("bn_guess", [P, V36])
        t_all = sb("bn_newton", [P, V36])
        rs_all = sb("bn_rstd", [P, V36])
        inv = sb("bn_scale", [P, CT])
        arow = sb("abn_scale", [P, HIDDEN])
        obias = sb("out_bias", [P, CT])
        wsum = sb("weight_abs_sums", [P, KERNELS])
        wsum1 = sb("weight_abs_sum", [P, 1])
        wtop = sb("weight_top", [1, 1])
        wall = sb("weight_top_all", [P, 1])
        wscale = sb("weight_scale", [P, 1])
        unscale = sb("weight_unscale", [P, 1])

        acc = [ctx.enter_context(nc.psum_tensor(f"product_{k}", [P, 512], f32)) for k in range(BANKS)]
        small = ctx.enter_context(nc.psum_tensor("small", [P, 512], f32))
        gmean_p, gvar_p, hid_p = small[:, 0:CT], small[:, 8:8 + CT], small[:, 256:256 + CT * HIDDEN]
        top_row, top_all = small[0:1, 64:64 + P], small[:, 200:201]

        y_free = y[:, :, :, :].rearrange("p a t n -> p (a t n)")[:, 0:CT * C]

        def p_(name):
            return pa[:, where[name][0]:where[name][1]]

        params_in = sem("params_in")
        weight_in = [sem(f"weight_in_{k}") for k in range(KERNELS)]
        chunk_in = [sem(f"chunk_in_{k}") for k in range(RING)]
        chunk_out = [sem(f"chunk_out_{k}") for k in range(RING)]
        order = sem("vector_order")
        stats_done = sem("stats_done")
        wsum_ready = sem("wsum_ready")
        catt_ready = sem("catt_ready")
        first_w_ready = sem("first_w_ready")
        wtop_ready = sem("wtop_ready")
        const_ready = sem("const_ready")
        means_ready = sem("means_ready")
        spread_ready = sem("spread_ready")
        var_ready = sem("var_ready")
        norm_ready = sem("norm_ready")
        pooled_ready = sem("pooled_ready")
        logits_ready = sem("logits_ready")
        att_ready = sem("att_ready")
        mix_ready = sem("mix_ready")
        first_mix_ready = sem("first_mix_ready")
        wlo_ready = sem("wlo_ready")
        lo_ready = sem("lo_ready")
        add_done = sem("add_done")
        ln_ready = sem("ln_ready")
        guess_ready = sem("guess_ready")
        exp_ready = sem("exp_ready")
        mix0_ready = sem("mix0_ready")
        whi_ready = sem("whi_ready")
        abs_done = sem("abs_done")
        first_whi_ready = sem("first_whi_ready")
        xn_ready = sem("xn_ready")
        hi_ready = sem("hi_ready")
        evac_done = sem("evac_done")
        mm_done = sem("mm_done")
        top_moved = sem("top_moved")
        gmean_done = sem("gmean_done")
        gvar_done = sem("gvar_done")
        hid_done = sem("hid_done")

        block = ctx.enter_context(nc.Block())

        NORM_AHEAD, SPLIT_AHEAD = 2, 1

        @block.sync
        def _(sp):
            def load(b, slot):
                n = slot % CHUNKS
                sp.dma_start(xs[:, slot], x_d[b, :, :, n * COLS:(n + 1) * COLS]).then_inc(chunk_in[slot], 16)

            sp.dma_start(pa[:, :], par).then_inc(params_in, 16)
            for slot in range(RING):
                if slot == CHUNKS + 2:
                    for k in range(KERNELS):
                        sp.dma_start(w[:, k], wt[:, k]).then_inc(weight_in[k], 16)
                load(slot // CHUNKS, slot)

            def body(i, last):
                turn = Turn(sp, i)
                for s in range(RING):
                    n = s % CHUNKS
                    b = 2 * i + s // CHUNKS
                    sp.wait_ge(add_done, turn.at(2 * RING, 4 + 2 * (s + 1)))
                    sp.dma_start(out_d[b, :, :, n * COLS:(n + 1) * COLS], xs[:, s]).then_inc(chunk_out[s], 16)
                    if not last:
                        sp.wait_ge(chunk_out[s], turn.at(16, 16))
                        load(b + 2, s)
            with sp.Fori(0, TURNS - 1) as i:
                body(i, False)
            body(TURNS - 1, True)
            for s in range(RING):
                sp.wait_ge(chunk_out[s], 16 * TURNS)

        @block.scalar
        def _(act):
            def norm(turn, f, t):
                u = f // CHUNKS % 2
                if t == 0:
                    act.wait_ge(norm_ready, turn.at(2, f // CHUNKS + 1))
                    if f >= 2 or not isinstance(turn.i, int):
                        act.wait_ge(lo_ready, turn.at(RING, f - 1))
                ins = nc.scalar.activation(xn[:, f % 2, t], xs[:, f % RING, t], ACT.Identity,
                                           bias=nbias[:, u, t:t + 1], scale=nscale[:, u, t:t + 1])
                if t == CT - 1:
                    ins.then_inc(xn_ready, 1)

            def split(turn, f):
                act.wait_ge(xn_ready, turn.at(RING, f + 1))
                nc.scalar.activation(xhi[:, f % 2], xn[:, f % 2], ACT.Copy).then_inc(hi_ready, 1)

            def evacuate(turn, s, t):
                k = 4 * s + t
                u = s // CHUNKS
                act.wait_ge(mm_done, turn.at(4 * RING, k + 1))
                if t % 2 == 0:
                    act.wait_ge(add_done, turn.at(2 * RING, 2 * s + t // 2 + 1))
                nc.scalar.activation(y[:, s % 2, t], acc[k % BANKS][:, 0:COLS], ACT.Identity,
                                     bias=obias[:, t:t + 1], scale=oscale[:, u, t:t + 1]).then_inc(evac_done, 1)

            def guess(turn, b):
                act.wait_ge(var_ready, turn.at(2, b + 1))
                nc.scalar.activation(ln[:, :], ve[:, :], ACT.Ln).then_inc(ln_ready, 1)
                act.wait_ge(ln_ready, turn.at(2, b + 2))
                nc.scalar.activation(r0[:, :], ln[:, :], ACT.Exp, scale=-0.5).then_inc(guess_ready, 1)

            def exponentials(turn, b):
                act.wait_ge(logits_ready, turn.at(2, b + 1))
                nc.scalar.activation(ez[:, :], z[:, :], ACT.Exp, scale=-1.0).then_inc(exp_ready, 1)

            def first_mix(turn, b):
                act.wait_ge(att_ready, turn.at(2, b + 1))
                if b or not isinstance(turn.i, int):
                    act.wait_ge(wlo_ready, turn.at(2, b))
                nc.scalar.activation(mix[:, :, :], w[:, 0], ACT.Copy, scale=katt[:, 0:1]).then_inc(mix0_ready, 1)

            def split_weight(turn, b):
                act.wait_ge(mix_ready, turn.at(2, b))
                for t in range(CT):
                    nc.scalar.activation(whi[:, b % 2, t], mix[:, t], ACT.Copy,
                                         scale=catt[:, t:t + 1]).then_inc(whi_ready, 1)

            act.preload_act_table_set("natural_log_exp_and_others")
            act.sem_inc(evac_done, BANKS)
            start = Turn(act, 0)
            act.wait_ge(const_ready, 2)
            nc.scalar.activation(ln_all[:, :], v_all[:, :], ACT.Ln).then_inc(ln_ready, 1)
            act.wait_ge(ln_ready, 1)
            nc.scalar.activation(r_all[:, :], ln_all[:, :], ACT.Exp, scale=-0.5).then_inc(guess_ready, 1)
            guess(start, 0)
            for t in range(CT):
                norm(start, 0, t)
            split(start, 0)
            for k in range(KERNELS):
                act.wait_ge(weight_in[k], 16)
                if k:
                    act.wait_ge(abs_done, k)
                nc.scalar.activation(y_free, w[:, k], ACT.Abs, accum_out=wsum[:, k:k + 1]).then_inc(abs_done, 1)
                if k == 0:
                    exponentials(start, 0)
                if k == 1:
                    first_mix(start, 0)
            for t in range(CT):
                norm(start, 1, t)
            act.wait_ge(catt_ready, 1)
            for o in range(CT):
                cols = slice(o * P, (o + 1) * P)
                act.wait_ge(first_mix_ready, o + 1)
                for t in range(CT):
                    ins = nc.scalar.activation(whi[:, 0, t, cols], mix[:, t, cols], ACT.Copy, scale=catt[:, t:t + 1])
                    ins.then_inc(whi_ready if o == 0 else first_whi_ready, 1)

            def body(i, last):
                turn = Turn(act, i)
                for s in range(RING):
                    n, b = s % CHUNKS, s // CHUNKS + 1
                    prepare = not (last and b == 2)
                    for t in range(CT):
                        if t == 0 and not (last and s + SPLIT_AHEAD >= RING):
                            split(turn, s + SPLIT_AHEAD)
                        evacuate(turn, s, t)
                        if not (last and s + NORM_AHEAD >= RING):
                            norm(turn, s + NORM_AHEAD, t)
                        if prepare:
                            if (n, t) == (3, 0):
                                guess(turn, b)
                            if (n, t) == (4, 0):
                                exponentials(turn, b)
                            if (n, t) == (4, 1):
                                first_mix(turn, b)
                            if (n, t) == (5, 2):
                                split_weight(turn, b)
            with act.Fori(0, TURNS - 1) as i:
                body(i, False)
            body(TURNS - 1, True)

        @block.vector
        def _(dve):
            done = [0]

            def step(ins):
                done[0] += 1
                ins.then_inc(order, 1)

            def after(turn):
                dve.wait_ge(order, turn.at(2 * STEPS, done[0]))

            STEPS = 24 + CT

            def stats(turn, f, t):
                if t == 0:
                    dve.wait_ge(chunk_in[f % RING], turn.at(16, 16 * (f // RING + 1)))
                ins = nc.vector.bn_stats(bst[:, f // CHUNKS % 2, t, f % CHUNKS], xs[:, f % RING, t])
                if t == CT - 1:
                    ins.then_inc(stats_done, 1)

            def split(turn, f):
                dve.wait_ge(hi_ready, turn.at(RING, f + 1))
                nc.vector.tensor_tensor(xlo[:, f % 2], xn[:, f % 2], xhi[:, f % 2], ALU.subtract).then_inc(lo_ready, 1)

            def add(turn, s, half):
                dve.wait_ge(evac_done, turn.at(4 * RING, BANKS + 4 * s + 2 * half + 2))
                two = slice(2 * half, 2 * half + 2)
                nc.vector.tensor_tensor(xs[:, s, two], xs[:, s, two], y[:, s % 2, two], ALU.add).then_inc(add_done, 1)

            def newton(turn, r, guess_, v, t):
                step(nc.vector.tensor_tensor(t, guess_, guess_, ALU.mult))
                after(turn)
                step(nc.vector.tensor_tensor(t, t, v, ALU.mult))
                after(turn)
                step(nc.vector.tensor_scalar(t, t, -0.5, 1.5, ALU.mult, ALU.add))
                after(turn)
                step(nc.vector.tensor_tensor(r, guess_, t, ALU.mult))
                after(turn)


            def stats_complete(turn, b):
                dve.wait_ge(stats_done, turn.at(RING, CHUNKS * (b + 1)))

            def channel_means(turn, b):
                for t in range(CT):
                    ins = nc.vector.bn_aggr(mv[:, t], bst[:, b % 2, t].rearrange("p c k -> p (c k)"))
                ins.then_inc(means_ready, 1)

            def group_spread(turn, b):
                dve.wait_ge(means_ready, turn.at(2, b + 1))
                dve.wait_ge(gmean_done, turn.at(2, b + 1))
                step(nc.vector.tensor_tensor(dev[:, :], mv[:, :, 0], gmean_p, ALU.subtract))
                step(nc.vector.tensor_copy(gm[:, :], gmean_p))
                after(turn)
                step(nc.vector.tensor_tensor(spread[:, :], dev[:, :], dev[:, :], ALU.mult))
                after(turn)
                nc.vector.tensor_tensor(spread[:, :], spread[:, :], mv[:, :, 1], ALU.add).then_inc(spread_ready, 1)

            def group_var(turn, b):
                dve.wait_ge(gvar_done, turn.at(2, b + 1))
                nc.vector.tensor_scalar(ve[:, :], gvar_p, GN_EPS, None, ALU.add).then_inc(var_ready, 1)

            def norms(turn, b):
                u = b % 2
                dve.wait_ge(guess_ready, turn.at(2, b + 2))
                newton(turn, rstd[:, :], r0[:, :], ve[:, :], tmp[:, :])
                step(nc.vector.tensor_scalar(nscale[:, u], rstd[:, :], X_SCALE, None, ALU.mult))
                step(nc.vector.tensor_tensor(pooled[:, :], dev[:, :], rstd[:, :], ALU.mult))
                after(turn)
                nc.vector.scalar_tensor_tensor(out=nbias[:, u], in0=gm[:, :], scalar=-1.0, in1=nscale[:, u],
                                               op0=ALU.mult, op1=ALU.mult).then_inc(norm_ready, 1)
                nc.vector.tensor_tensor(fcp[:, :, :], p_("fc").rearrange("p (t a) -> p t a", t=CT),
                                        pooled[:, :].unsqueeze(2).to_broadcast([P, CT, HIDDEN]),
                                        ALU.mult).then_inc(pooled_ready, 1)

            def logits(turn, b):
                dve.wait_ge(hid_done, turn.at(2, b + 1))
                step(nc.vector.tensor_reduce(hid[:, :], hid_p.rearrange("p (t a) -> p a t", a=HIDDEN), AX.X, ALU.add))
                after(turn)
                step(nc.vector.tensor_tensor(hid[:, :], hid[:, :], p_("abn_m"), ALU.subtract))
                after(turn)
                step(nc.vector.tensor_tensor(hid[:, :], hid[:, :], arow[:, :], ALU.mult))
                after(turn)
                step(nc.vector.tensor_tensor(hid[:, :], hid[:, :], p_("abn_b"), ALU.add))
                after(turn)
                step(nc.vector.scalar_tensor_tensor(out=prod[:, :, :],
                                                    in0=hid[:, :].unsqueeze(1).to_broadcast([P, HEADS, HIDDEN]),
                                                    scalar=0.0, in1=p_("heads").rearrange("p (j a) -> p j a", a=HIDDEN),
                                                    op0=ALU.max, op1=ALU.mult))
                after(turn)
                step(nc.vector.tensor_reduce(z[:, :], prod[:, :, :], AX.X, ALU.add))
                after(turn)
                step(nc.vector.tensor_tensor(z[:, :], z[:, :], p_("head_bias"), ALU.add))
                after(turn)
                step(nc.vector.reduce_max(kmax[:, :], z[:, 2 * CT:HEADS], AX.X))
                after(turn)
                nc.vector.tensor_scalar(z[:, 2 * CT:HEADS], z[:, 2 * CT:HEADS], kmax[:, 0:1], -1.0,
                                        ALU.subtract, ALU.mult).then_inc(logits_ready, 1)

            def attentions(turn, b):
                dve.wait_ge(exp_ready, turn.at(2, b + 1))
                step(nc.vector.tensor_scalar(sig[:, :], ez[:, 0:2 * CT], 1.0, None, ALU.add))
                step(nc.vector.reduce_sum(ksum[:, :], ez[:, 2 * CT:HEADS], AX.X))
                after(turn)
                step(nc.vector.reciprocal(sig[:, :], sig[:, :]))
                step(nc.vector.reciprocal(ksum[:, :], ksum[:, :]))
                after(turn)
                nc.vector.tensor_scalar(katt[:, :], ez[:, 2 * CT:HEADS], ksum[:, 0:1], None,
                                        ALU.mult).then_inc(att_ready, 1)

            def scaled_attentions(turn, b):
                after(turn)
                step(nc.vector.tensor_tensor(oscale[:, b % 2], sig[:, CT:2 * CT], inv[:, :], ALU.mult))
                return nc.vector.tensor_scalar(catt[:, :], sig[:, 0:CT], wscale[:, 0:1], None, ALU.mult)

            def mix_kernel(turn, b, k):
                if k == 1:
                    dve.wait_ge(att_ready, turn.at(2, b + 1))
                    dve.wait_ge(mix0_ready, turn.at(2, b + 1))
                else:
                    after(turn)
                ins = nc.vector.scalar_tensor_tensor(out=mix[:, :, :], in0=w[:, k], scalar=katt[:, k:k + 1],
                                                     in1=mix[:, :, :], op0=ALU.mult, op1=ALU.add)
                if k == KERNELS - 1:
                    ins.then_inc(mix_ready, 1)
                else:
                    step(ins)

            def split_weight(turn, b, t):
                if t == 0:
                    dve.wait_ge(mix_ready, turn.at(2, b))
                dve.wait_ge(whi_ready, turn.at(2 * CT, CT * b + t + 1))
                ins = nc.vector.scalar_tensor_tensor(out=wlo[:, b % 2, t], in0=mix[:, t], scalar=catt[:, t:t + 1],
                                                     in1=whi[:, b % 2, t], op0=ALU.mult, op1=ALU.subtract)
                if t == CT - 1:
                    ins.then_inc(wlo_ready, 1)
                else:
                    step(ins)

            start = Turn(dve, 0)
            dve.sem_inc(add_done, 4)
            nc.vector.memset(ones[:, :], 1.0).then_inc(const_ready, 1)
            dve.wait_ge(params_in, 16)
            nc.vector.tensor_scalar(v_all[:, :], pa[:, where["bn_v"][0]:where["abn_v"][1]], BN_EPS, None,
                                    ALU.add).then_inc(const_ready, 1)
            dve.wait_ge(guess_ready, 1)
            newton(start, rs_all[:, :], r_all[:, :], v_all[:, :], t_all[:, :])
            step(nc.vector.tensor_tensor(inv[:, :], p_("bn_g"), rs_all[:, 0:CT], ALU.mult))
            step(nc.vector.tensor_tensor(arow[:, :], p_("abn_g"), rs_all[:, CT:V36], ALU.mult))
            after(start)
            step(nc.vector.tensor_tensor(obias[:, :], p_("bn_m"), inv[:, :], ALU.mult))
            after(start)
            step(nc.vector.tensor_tensor(obias[:, :], p_("bn_b"), obias[:, :], ALU.subtract))
            for f in range(CHUNKS):
                for t in range(CT):
                    stats(start, f, t)
            stats_complete(start, 0)
            channel_means(start, 0)
            group_spread(start, 0)
            for t in range(CT):
                stats(start, CHUNKS, t)
            group_var(start, 0)
            stats(start, CHUNKS + 1, 0)
            norms(start, 0)
            stats(start, CHUNKS + 1, 1)
            stats(start, CHUNKS + 1, 2)
            logits(start, 0)
            stats(start, CHUNKS + 1, 3)
            attentions(start, 0)
            split(start, 0)

            def first_mix(o):
                cols = slice(o * P, (o + 1) * P)
                if o == 0:
                    dve.wait_ge(att_ready, 1)
                    dve.wait_ge(mix0_ready, 1)
                for k in range(1, KERNELS):
                    if k > 1:
                        after(start)
                    if o == 0:
                        dve.wait_ge(weight_in[k], 16)
                    ins = nc.vector.scalar_tensor_tensor(out=mix[:, :, cols], in0=w[:, k, :, cols],
                                                         scalar=katt[:, k:k + 1], in1=mix[:, :, cols],
                                                         op0=ALU.mult, op1=ALU.add)
                    if k == KERNELS - 1:
                        ins.then_inc(first_mix_ready, 1)
                    else:
                        step(ins)

            def first_split(o):
                cols = slice(o * P, (o + 1) * P)
                dve.wait_ge(first_mix_ready, o + 1)
                for t in range(CT):
                    if o == 0:
                        dve.wait_ge(whi_ready, t + 1)
                    else:
                        dve.wait_ge(first_whi_ready, CT * (o - 1) + t + 1)
                    ins = nc.vector.scalar_tensor_tensor(out=wlo[:, 0, t, cols], in0=mix[:, t, cols],
                                                         scalar=catt[:, t:t + 1], in1=whi[:, 0, t, cols],
                                                         op0=ALU.mult, op1=ALU.subtract)
                    if t == CT - 1:
                        ins.then_inc(first_w_ready, 1)
                    elif (o, t) == (0, 0):
                        ins.then_inc(wlo_ready, 1)
                    else:
                        step(ins)

            first_mix(0)
            first_mix(1)
            dve.wait_ge(abs_done, KERNELS)
            nc.vector.reduce_sum(wsum1[:, :], wsum[:, :], AX.X).then_inc(wsum_ready, 1)
            dve.wait_ge(top_moved, 1)
            nc.vector.reduce_max(wtop[:, :], top_row, AX.X).then_inc(wtop_ready, 1)
            dve.wait_ge(top_moved, 2)
            step(nc.vector.tensor_scalar(wall[:, :], top_all, 1e-30, None, ALU.max))
            after(start)
            step(nc.vector.reciprocal(wscale[:, :], wall[:, :]))
            step(nc.vector.tensor_scalar(unscale[:, :], wall[:, :], 1.0 / (W_TOP * X_SCALE), None, ALU.mult))
            after(start)
            step(nc.vector.tensor_scalar(wscale[:, :], wscale[:, :], W_TOP, None, ALU.mult))
            step(nc.vector.tensor_scalar(inv[:, :], inv[:, :], unscale[:, 0:1], None, ALU.mult))
            scaled_attentions(start, 0).then_inc(catt_ready, 1)
            dve.wait_ge(catt_ready, 1)
            for o in range(CT):
                if o > 1:
                    first_mix(o)
                first_split(o)
            for t in range(CT):
                stats(start, CHUNKS + 2, t)
            before = done[0]

            def stats_at(s, t):
                u, n = divmod(s, CHUNKS)
                near, far = CHUNKS * (u + 1), CHUNKS * (u + 2)
                whole = {(0, 0): near + 3, (0, 2): near + 4, (1, 0): near + 5, (1, 3): near + 6,
                         (2, 2): far, (4, 0): far + 1, (6, 2): far + 2}
                return [(whole[n, t], tile) for tile in range(CT)] if (n, t) in whole else []

            def body(i, last):
                turn = Turn(dve, i)
                done[0] = before
                for s in range(RING):
                    n, b = s % CHUNKS, s // CHUNKS + 1
                    prepare = not (last and b == 2)
                    for t in range(CT):
                        if t == 0 and s:
                            if prepare and n == 2:
                                stats_complete(turn, b)
                            add(turn, s - 1, 1)
                        for f, tile in stats_at(s, t):
                            if not (last and f >= RING):
                                stats(turn, f, tile)
                        if prepare and (n, t) == (3, 1):
                            norms(turn, b)
                        if prepare and (n, t) == (4, 1):
                            attentions(turn, b)
                            step(scaled_attentions(turn, b))
                        if t == 1 and not (last and s + SPLIT_AHEAD >= RING):
                            split(turn, s + SPLIT_AHEAD)
                        if t == 2:
                            add(turn, s, 0)
                        if prepare:
                            if (n, t) == (2, 0):
                                channel_means(turn, b)
                            if (n, t) == (2, 1):
                                group_spread(turn, b)
                            if (n, t) == (3, 0):
                                group_var(turn, b)
                            if (n, t) == (3, 3):
                                logits(turn, b)
                            if (n, t) in ((4, 2), (5, 0), (5, 1)):
                                mix_kernel(turn, b, {(4, 2): 1, (5, 0): 2, (5, 1): 3}[n, t])
                            if (n, t) in ((5, 3), (6, 0)):
                                for j in {3: (0, 1), 0: (2, 3)}[t]:
                                    split_weight(turn, b, j)
                    if s == CHUNKS - 1:
                        assert done[0] - before == STEPS, done[0] - before
                add(turn, RING - 1, 1)
            with dve.Fori(0, TURNS - 1) as i:
                body(i, False)
            body(TURNS - 1, True)

        @block.tensor
        def _(pe):
            def group_mean(turn, b):
                pe.wait_ge(means_ready, turn.at(2, b + 1))
                nc.tensor.matmul(gmean_p, p_("group"), mv[:, :, 0], start=True, stop=True).then_inc(gmean_done, 1)

            def group_var(turn, b):
                pe.wait_ge(spread_ready, turn.at(2, b + 1))
                nc.tensor.matmul(gvar_p, p_("group"), spread[:, :], start=True, stop=True).then_inc(gvar_done, 1)

            def hidden(turn, b):
                pe.wait_ge(pooled_ready, turn.at(2, b + 1))
                nc.tensor.matmul(hid_p, ones[:, :], fcp[:, :, :].rearrange("p t a -> p (t a)"),
                                 start=True, stop=True).then_inc(hid_done, 1)

            start = Turn(pe, 0)
            pe.wait_ge(params_in, 16)
            pe.wait_ge(const_ready, 1)
            group_mean(start, 0)
            group_var(start, 0)
            hidden(start, 0)
            pe.wait_ge(wsum_ready, 1)
            nc.tensor.matmul(top_row, wsum1[:, 0:1], p_("ident"), start=True, stop=True).then_inc(top_moved, 1)
            pe.wait_ge(wtop_ready, 1)
            nc.tensor.matmul(top_all, ones[0:1, :], wtop[0:1, 0:1], start=True, stop=True).then_inc(top_moved, 1)

            def product(turn, s, o):
                k = 4 * s + o
                u = s // CHUNKS
                if o == 0:
                    if s % CHUNKS == 0:
                        pe.wait_ge(wlo_ready, turn.at(2, u + 1))
                    pe.wait_ge(lo_ready, turn.at(RING, s + 1))
                if s == 0:
                    pe.wait_ge(first_w_ready, o + 1)
                pe.wait_ge(evac_done, turn.at(4 * RING, k + 1))
                bank = acc[k % BANKS][:, 0:COLS]
                cols = slice(o * P, (o + 1) * P)
                for t in range(CT):
                    hi, lo = xhi[:, s % 2, t], xlo[:, s % 2, t]
                    nc.tensor.matmul(bank, whi[:, u, t, cols], hi, start=(t == 0), stop=False)
                    nc.tensor.matmul(bank, whi[:, u, t, cols], lo, start=False, stop=False)
                    ins = nc.tensor.matmul(bank, wlo[:, u, t, cols], hi, start=False, stop=(t == CT - 1))
                ins.then_inc(mm_done, 1)

            def body(i, last):
                turn = Turn(pe, i)
                for s in range(RING):
                    n, b = s % CHUNKS, s // CHUNKS + 1
                    prepare = not (last and b == 2)
                    for o in range(CT):
                        product(turn, s, o)
                        if prepare and (n, o) == (2, 1):
                            group_mean(turn, b)
                        if prepare and (n, o) == (2, 3):
                            group_var(turn, b)
                        if prepare and (n, o) == (3, 2):
                            hidden(turn, b)
            with pe.Fori(0, TURNS - 1) as i:
                body(i, False)
            body(TURNS - 1, True)


def kernel(x, L0_conv_fc_w, L0_conv_abn_g, L0_conv_abn_b, L0_conv_abn_m, L0_conv_abn_v, L0_conv_ch_w, L0_conv_ch_b,
           L0_conv_fl_w, L0_conv_fl_b, L0_conv_kn_w, L0_conv_kn_b, L0_conv_weight, L0_conv_bn_g, L0_conv_bn_b,
           L0_conv_bn_m, L0_conv_bn_v):
    import numpy as np
    import concourse.bacc as bacc
    from concourse.bass_utils import run_bass_kernel_spmd

    x = np.asarray(x)
    B, C, H, W = x.shape
    CT = C // P
    where, n_par = columns(CT)
    f = np.float32
    par = np.zeros((P, n_par), f)

    def put(name, a):
        a = np.asarray(a)
        lo, hi = where[name]
        par[:, lo:hi] = a.reshape(-1, hi - lo)

    def by_channel(a):
        a = np.asarray(a)
        return np.swapaxes(a.reshape(CT, P, *a.shape[1:]), 0, 1)

    def everywhere(a):
        a = np.asarray(a)
        return np.broadcast_to(a, (P, *a.shape))

    put("fc", by_channel(np.asarray(L0_conv_fc_w).T))
    put("heads", np.concatenate([by_channel(L0_conv_ch_w), by_channel(L0_conv_fl_w), everywhere(L0_conv_kn_w)], 1))
    put("head_bias", np.concatenate([by_channel(L0_conv_ch_b), by_channel(L0_conv_fl_b), everywhere(L0_conv_kn_b)], 1))
    for name, a in (("g", L0_conv_abn_g), ("b", L0_conv_abn_b), ("m", L0_conv_abn_m), ("v", L0_conv_abn_v)):
        put("abn_" + name, everywhere(a))
    for name, a in (("g", L0_conv_bn_g), ("b", L0_conv_bn_b), ("m", L0_conv_bn_m), ("v", L0_conv_bn_v)):
        put("bn_" + name, by_channel(a))
    put("group", np.kron(np.eye(P // GROUP, dtype=f), np.full((GROUP, GROUP), 1.0 / GROUP, f)))
    put("ident", np.eye(P, dtype=f))
    wt = np.ascontiguousarray(np.asarray(L0_conv_weight).reshape(KERNELS, C, CT, P).transpose(3, 0, 2, 1))

    nc = bacc.Bacc("TRN2", target_bir_lowering=False, num_devices=1)
    arrays = {"x": np.ascontiguousarray(x.reshape(B, C, H * W)), "wt": wt, "par": par}
    args = [nc.dram_tensor(n, a.shape, mybir.dt.from_np(a.dtype), kind="ExternalInput").ap() for n, a in arrays.items()]
    out = nc.dram_tensor("out", (B, C, H * W), mybir.dt.float32, kind="ExternalOutput").ap()
    build(nc, *args, out)
    r = run_bass_kernel_spmd(nc, [arrays], core_ids=[0])
    return r.results[0]["out"].reshape(B, C, H, W)
```
